# Optimizing a Trainium2 kernel written in Bass

```python
import numpy as np
import jax
import jax.numpy as jnp

def _softmax(x, axis=-1):
    return jax.nn.softmax(x, axis=axis)

def _gelu(x):
    return jax.nn.gelu(x, approximate=True)

def _silu(x):
    return jax.nn.silu(x)

def _sigmoid(x):
    return jax.nn.sigmoid(x)

def _layernorm(x, axis=-1, eps=1e-05):
    m = jnp.mean(x, axis=axis, keepdims=True)
    v = jnp.var(x, axis=axis, keepdims=True)
    return (x - m) / jnp.sqrt(v + eps)

def _scatter_add(tgt, idx, src, axis=0):
    return tgt.at[idx].add(src)

def _segment_sum(src, seg, n):
    return jax.ops.segment_sum(src, seg, n)
kernel_name = 'mk_prb_d1_jaxref_r8_2b400a'

def setup_inputs(seed: int=0):
    np.random.seed(seed)
    _w = jnp.asarray

    def _L0_attn_setup():
        import jax, jax.numpy as jnp
        import numpy as np
        B, S, D, H, F = (4, 1024, 128, 16, 64)
        DK = D // H
        EPS = 1e-06

        def _heads(x, W, b):
            y = jnp.einsum('bsd,de->bse', x, W) + b
            return y.reshape(x.shape[0], x.shape[1], H, DK).transpose(0, 2, 1, 3)
        key = jax.random.key(seed)
        ks = jax.random.split(key, 6)
        scale = 1.0 / np.sqrt(D)
        x = jax.random.normal(ks[0], (B, S, D), dtype=jnp.float32)
        Wq = jax.random.normal(ks[1], (D, D), dtype=jnp.float32) * scale
        Wk = jax.random.normal(ks[2], (D, D), dtype=jnp.float32) * scale
        Wv = jax.random.normal(ks[3], (D, D), dtype=jnp.float32) * scale
        Wo = jax.random.normal(ks[4], (D, D), dtype=jnp.float32) * scale
        rw = jax.random.normal(ks[5], (H, DK, F), dtype=jnp.float32) / np.sqrt(DK)
        zb = jnp.zeros((D,), dtype=jnp.float32)
        return {'x': x, 'Wq': Wq, 'bq': zb, 'Wk': Wk, 'bk': zb, 'Wv': Wv, 'bv': zb, 'Wo': Wo, 'bo': zb, 'rw': rw}
    _L0_attn_in = _L0_attn_setup()

    def _L0_ffn_setup():
        import jax, jax.numpy as jnp
        import numpy as np
        E, H, I = (8, 128, 512)
        B, S = (4, 256)
        key = jax.random.key(seed)
        k0, k1, k2, k3 = jax.random.split(key, 4)
        s = 0.02
        return {'hidden_states': jax.random.normal(k0, (B, S, H), dtype=jnp.float32), 'w1': jax.random.normal(k1, (E, H, I), dtype=jnp.float32) * s, 'b1': jnp.zeros((E, I), dtype=jnp.float32), 'w2': jax.random.normal(k2, (E, I, H), dtype=jnp.float32) * s, 'b2': jnp.zeros((E, H), dtype=jnp.float32), 'wr': jax.random.normal(k3, (H, E), dtype=jnp.float32) * s, 'br': jnp.zeros((E,), dtype=jnp.float32)}
    _L0_ffn_in = _L0_ffn_setup()
    _d = {'L0_attn_x': _L0_attn_in['x'], 'L0_attn_Wq': _L0_attn_in['Wq'], 'L0_attn_bq': _L0_attn_in['bq'], 'L0_attn_Wk': _L0_attn_in['Wk'], 'L0_attn_bk': _L0_attn_in['bk'], 'L0_attn_Wv': _L0_attn_in['Wv'], 'L0_attn_bv': _L0_attn_in['bv'], 'L0_attn_Wo': _L0_attn_in['Wo'], 'L0_attn_bo': _L0_attn_in['bo'], 'L0_attn_rw': _L0_attn_in['rw'], 'L0_ffn_w1': _L0_ffn_in['w1'], 'L0_ffn_b1': _L0_ffn_in['b1'], 'L0_ffn_w2': _L0_ffn_in['w2'], 'L0_ffn_b2': _L0_ffn_in['b2'], 'L0_ffn_wr': _L0_ffn_in['wr'], 'L0_ffn_br': _L0_ffn_in['br']}
    _x0 = _d['L0_attn_x']
    _d['L0_attn_x'] = jax.random.normal(jax.random.fold_in(jax.random.key(seed), 1), (16, 256, 128), dtype=_x0.dtype)
    del _x0
    return _d

def reference(L0_attn_x, L0_attn_Wq, L0_attn_bq, L0_attn_Wk, L0_attn_bk, L0_attn_Wv, L0_attn_bv, L0_attn_Wo, L0_attn_bo, L0_attn_rw, L0_ffn_w1, L0_ffn_b1, L0_ffn_w2, L0_ffn_b2, L0_ffn_wr, L0_ffn_br):

    def _L0_attn_ref(x, Wq, bq, Wk, bk, Wv, bv, Wo, bo, rw):
        import jax, jax.numpy as jnp
        import numpy as np
        B, S, D, H, F = (4, 1024, 128, 16, 64)
        DK = D // H
        EPS = 1e-06

        def _heads(x, W, b):
            y = jnp.einsum('bsd,de->bse', x, W) + b
            return y.reshape(x.shape[0], x.shape[1], H, DK).transpose(0, 2, 1, 3)
        q = _heads(x, Wq, bq)
        k = _heads(x, Wk, bk)
        v = _heads(x, Wv, bv)
        qp = jax.nn.relu(jnp.einsum('bhsd,hdf->bhsf', q, rw)) + EPS
        kp = jax.nn.relu(jnp.einsum('bhsd,hdf->bhsf', k, rw)) + EPS
        kv = jnp.einsum('bhsf,bhsd->bhfd', kp, v)
        qkv = jnp.einsum('bhsf,bhfd->bhsd', qp, kv)
        norm = jnp.einsum('bhsf,bhf->bhs', qp, kp.sum(axis=2))
        out = qkv / (norm[..., None] + EPS)
        out = out.transpose(0, 2, 1, 3).reshape(x.shape[0], x.shape[1], D)
        return jnp.einsum('bsd,de->bse', out, Wo) + bo

    def _L0_ffn_ref(hidden_states, w1, b1, w2, b2, wr, br):
        import jax, jax.numpy as jnp
        import numpy as np
        E, H, I = (8, 128, 512)
        B, S = (4, 256)
        b, s, h = hidden_states.shape
        x = hidden_states.reshape(-1, h)
        logits = x @ wr + br
        probs = jax.nn.softmax(logits, axis=-1)
        top_p, top_i = jax.lax.top_k(probs, 2)
        gate = top_p[:, 0] / (top_p[:, 0] + top_p[:, 1])
        top1 = top_i[:, 0]
        out = jnp.zeros_like(x)
        n_experts = w1.shape[0]
        for e in range(n_experts):
            hmid = jax.nn.gelu(x @ w1[e] + b1[e], approximate=False)
            hout = hmid @ w2[e] + b2[e]
            mask = top1 == e
            out = out + jnp.where(mask[:, None], hout * gate[:, None], 0.0)
        return out.reshape(b, s, h)
    x = L0_attn_x
    xn = _layernorm(x, axis=-1)
    x = x + _L0_attn_ref(xn, L0_attn_Wq, L0_attn_bq, L0_attn_Wk, L0_attn_bk, L0_attn_Wv, L0_attn_bv, L0_attn_Wo, L0_attn_bo, L0_attn_rw) + _L0_ffn_ref(xn, L0_ffn_w1, L0_ffn_b1, L0_ffn_w2, L0_ffn_b2, L0_ffn_wr, L0_ffn_br)
    return x

_drawn_inputs = setup_inputs


def setup_inputs(seed=0):
    import zlib

    import numpy as np

    out = dict(_drawn_inputs(seed))
    spreads = {'L0_attn_bq': (0.0, 0.8),
     'L0_attn_bk': (0.0, 0.8),
     'L0_attn_bv': (0.0, 0.1),
     'L0_attn_bo': (0.0, 0.1),
     'L0_ffn_b1': (0.0, 0.636),
     'L0_ffn_b2': (0.0, 0.1),
     'L0_ffn_br': (0.0, 0.1)}
    factors = {}
    for name, (base, spread) in spreads.items():
        noise = np.random.default_rng([zlib.crc32(name.encode()), seed]).standard_normal(out[name].shape)
        drawn = base * np.exp(spread * noise) if base else spread * noise
        out[name] = jnp.asarray(drawn.astype(out[name].dtype))
    for name, factor in factors.items():
        out[name] = (out[name] * factor).astype(out[name].dtype)
    return out
```

```python
from contextlib import ExitStack

import concourse.bass as bass
from concourse import mybir

F32 = mybir.dt.float32
F32R = mybir.dt.float32r
BF16 = mybir.dt.bfloat16
I32 = mybir.dt.int32
ALU = mybir.AluOpType
ACT = mybir.ActivationFunctionType
AX = mybir.AxisListType

P = 128
D = 128
NBATCH, S = 16, 256
K = S // P
TILES = NBATCH * K
ROWS = NBATCH * S
H, DK, F = 16, 8, 64
G = 4
GH = H // G
GD = GH * DK
NC = H * F // P
HD = D // NC
E, I = 8, 512
IB = I // P
SLOT_TILES = TILES + E - 1
XW = D + 2
CHUNK = 2
CHUNKS = NBATCH // CHUNK
RING = 3
VW = D + E
STAGE = 1024
SUMS = 4
STACK_LOADS = 16 * 8
R_GATE, R_EARLIER = 2, 8
LN_EPS = 1e-5
EPS = 1e-6


def build(nc, x, Wq, bq, Wk, bk, Wv, bv, Wo, bo, rw, w1, b1, w2, b2, wr, br, out):
    ctx = ExitStack()
    with ctx:
        def sb(name, shape, dt):
            return ctx.enter_context(nc.sbuf_tensor(name, shape, dt))

        def sem(name):
            return ctx.enter_context(nc.semaphore(name))

        q_parts = nc.dram_tensor("q_parts", [NBATCH, 2, P, S], F32, kind="Internal").ap()
        k_parts = nc.dram_tensor("k_parts", [NBATCH, 2, P, S], F32, kind="Internal").ap()
        sorted_x = nc.dram_tensor("sorted_x", [SLOT_TILES * P, XW], F32, kind="Internal").ap()
        expert_y = nc.dram_tensor("expert_y", [ROWS, D], F32, kind="Internal").ap()

        ident = sb("ident", [P, P], F32)
        before = sb("before", [P, P], BF16)
        ones_b = sb("ones_b", [P, P], BF16)
        ones_f = sb("ones_f", [P, XW], F32)
        ones_r = sb("ones_r", [P, P], F32R)
        wq_sb = sb("wq_sb", [P, D], F32)
        wk_sb = sb("wk_sb", [P, D], F32)
        wvr_sb = sb("wvr_sb", [P, VW], F32)
        wo_sb = sb("wo_sb", [P, D], F32)
        bq_col = sb("bq_col", [P, 1], F32)
        bk_col = sb("bk_col", [P, 1], F32)
        bias_vro = sb("bias_vro", [P, VW + D], BF16)
        bias_vr, bias_o = bias_vro[:, 0:VW], bias_vro[:, VW:VW + D]
        bias_f = sb("bias_f", [P, VW + D], F32)
        b2_rows = sb("b2_rows", [P, E * D], BF16)
        b1_rows = sb("b1_rows", [P, E * I], F32R)
        w1_hi = sb("w1_hi", [P, E * I], F32R)
        w1_lo = sb("w1_lo", [P, E * I], F32R)
        rw_stack = sb("rw_stack", [P, G, GH * F], F32R)
        head_mask = sb("head_mask", [P, P], F32)
        head_bit_i = sb("head_bit_i", [P, 1], I32)
        head_bit = sb("head_bit", [P, 1], F32)

        rows_all = sb("rows_all", [P, TILES, XW], F32)
        w2_sb = rows_all[:, :, :].rearrange("p t w -> p (t w)")[:, 0:E * IB * D]
        v_all = sb("v_all", [P, NBATCH, K * D], F32)
        y_all = v_all
        r_all = sb("r_all", [P, NBATCH, K * D], F32)

        arena = sb("arena", [P, 2 * NC * S], F32)
        q_feat = [arena[:, n * NC * S:(n + 1) * NC * S].rearrange("p (c n) -> p c n", c=NC) for n in range(2)]
        SX = CHUNK * K * D

        def part_of_arena(n):
            return arena[:, n * SX:(n + 1) * SX]

        x_ring = [part_of_arena(s) for s in range(2)]
        xn_ring = [part_of_arena(2 + s) for s in range(2)]
        xnT = [part_of_arena(4 + s) for s in range(2)]
        rw_f = arena[:, 6 * SX:8 * SX].rearrange("p (g n) -> p g n", g=G)
        arena_r = sb("arena_r", [P, 8, CHUNK * S], F32R)
        qk_part = [[[arena_r[:, 4 * n + 2 * h + s, :] for s in range(2)] for h in range(2)] for n in range(2)]
        stats = sb("stats", [P, CHUNK * K, 6], F32)
        meanvar = [sb(f"meanvar{s}", [P, CHUNK * K, 2], F32) for s in range(2)]
        ln_eps = sb("ln_eps", [P, 1], F32)
        std = [sb(f"std{s}", [P, CHUNK * K], F32) for s in range(2)]
        rstd = [sb(f"rstd{s}", [P, CHUNK * K], F32) for s in range(2)]

        logits = sb("logits", [P, TILES, E], F32)
        top8 = sb("top8", [P, TILES, E], F32)
        is_top = sb("is_top", [P, TILES, E], F32)
        rank_w = sb("rank_w", [P, TILES, E], F32)
        rank_i = sb("rank_i", [P, TILES, E], I32)
        top_w = sb("top_w", [P, TILES], F32)
        onehot = sb("onehot", [P, E, TILES], BF16)
        keep = sb("keep", [P, E, TILES], BF16)
        upto = sb("upto", [P, E, TILES], BF16)
        earlier = sb("earlier", [P, E, TILES], BF16)
        cnt_i = sb("cnt_i", [P, E], I32)
        tiles_i = sb("tiles_i", [P, E], I32)
        tiles_f = sb("tiles_f", [P, E], F32)
        tiles_upto = sb("tiles_upto", [P, E], F32)
        first_slot = sb("first_slot", [P, E], F32)
        place_a = sb("place_a", [P, E, TILES], F32)
        place_b = sb("place_b", [P, E, TILES], F32)
        place_f = sb("place_f", [P, TILES], F32)
        place_i = sb("place_i", [P, TILES], I32)
        slot_no_i = sb("slot_no_i", [P, SLOT_TILES], I32)
        slot_no = sb("slot_no", [P, SLOT_TILES], F32)
        passed = sb("passed", [P, SLOT_TILES, E], F32)
        expert_f = sb("expert_f", [P, SLOT_TILES], F32)
        expert_no = sb("expert_no", [P, SLOT_TILES], I32)
        gate_d = sb("gate_d", [P, TILES], F32)
        gate_e = sb("gate_e", [P, TILES], F32)
        gate_s = sb("gate_s", [P, TILES], F32)

        q_stack, k_stack = ([arena_r[:, 4 * n + 2 * s:4 * n + 2 * s + 2, :].rearrange("p a n -> p (a n)")
                             .rearrange("p (g n) -> p g n", g=G) for s in range(2)] for n in range(2))
        v_ones = [sb(f"v_ones{s}", [P, K, NC, 2 * HD], F32) for s in range(2)]
        k_feat = [sb(f"k_feat{s}", [P, K, NC, P + 1], F32) for s in range(2)]
        kv_T = sb("kv_T", [P, 2, P], F32)
        kv_num = [sb(f"kv_num{s}", [P, NC, GD], F32) for s in range(2)]
        kv_den = [sb(f"kv_den{s}", [P, NC, GD], F32) for s in range(2)]
        den = [sb(f"den{s}", [P, S], F32) for s in range(2)]
        num = [sb(f"num{s}", [P, S], F32) for s in range(2)]
        inv_den = sb("inv_den", [P, S], F32)
        attn_T = [sb(f"attn_T{s}", [P, S], F32) for s in range(2)]

        slot_rows = [sb(f"slot_rows{u}", [P, XW], F32) for u in range(RING)]
        xsT_hi = [sb(f"xsT_hi{u}", [P, P], F32R) for u in range(RING)]
        xsT_lo = [sb(f"xsT_lo{u}", [P, P], F32R) for u in range(RING)]
        hidden_all = sb("hidden_all", [P, 2 * RING * I], F32)
        hidden = [hidden_all[:, u * I:(u + 1) * I] for u in range(RING)]
        hidden_T = [hidden_all[:, (RING + u) * I:(RING + u + 1) * I] for u in range(RING)]
        stage = [hidden_all[:, s * STAGE:(s + 1) * STAGE] for s in range(2)]
        gate_id = sb("gate_id", [P, SLOT_TILES, 2], F32)
        row_id = [sb(f"row_id{u}", [P, 1], F32) for u in range(RING)]
        y_gated = [sb(f"y_gated{u}", [P, D], F32) for u in range(RING)]

        pair = [ctx.enter_context(nc.psum_tensor(f"pair{n}", [P, 1024], F32)) for n in range(2)]
        one = [ctx.enter_context(nc.psum_tensor(f"one{n}", [P, 512], F32)) for n in range(4)]
        xnT_bank = pair[0][:, 0:512]
        q_bank, k_bank = pair[0][:, 512:1024], pair[1][:, 0:512]
        v_bank = [one[n][:, 0:K * VW].rearrange("p (k n) -> p k n", k=K) for n in range(2)]
        rank_bank = one[3][:, 0:E * TILES].rearrange("p (e t) -> p e t", e=E)
        count_bank = one[2][:, 0:E]
        kv_bank = one[0][:, 0:2 * (P + 1)].rearrange("p (a n) -> p a n", a=2)
        kvT_bank = one[1][:, 0:2 * P].rearrange("p (a n) -> p a n", a=2)
        o_bank, wo_bank = one[2], one[3]
        hid_bank = [pair[0][:, 0:512], pair[0][:, 512:1024], pair[1][:, 0:512]]
        hidT_bank = [pair[1][:, 512:1024], one[0][:, :], one[1][:, :]]
        xsT_bank, y_bank = one[2][:, 0:P], one[3][:, 0:D]

        wts_in = sem("wts_in")
        bias_in = sem("bias_in")
        rw_in = sem("rw_in")
        bias_split, bias_ready = sem("bias_split"), sem("bias_ready")
        ones_ready = sem("ones_ready")
        rw_split, rw_ready = sem("rw_split"), sem("rw_ready")
        zeroed = sem("zeroed")
        pool_step = sem("pool_step")
        consts_ready = sem("consts_ready")
        mask_ready = sem("mask_ready")
        stage_in = sem("stage_in")
        experts_ready = sem("experts_ready")
        w2_in = sem("w2_in")
        filled = sem("filled")
        eps_ready, std_ready = sem("eps_ready"), sem("std_ready")
        x_loaded = [sem(f"x_loaded{s}") for s in range(2)]
        stats_ready, mv_ready, rstd_ready = sem("stats_ready"), sem("mv_ready"), sem("rstd_ready")
        xn_ready = sem("xn_ready")
        rows_saved = [sem(f"rows_saved{s}") for s in range(2)]
        xnT_ps, xnT_ready = sem("xnT_ps"), sem("xnT_ready")
        qk_ps, v_ps = sem("qk_ps"), sem("v_ps")
        hi_ready, lo_ready = sem("hi_ready"), sem("lo_ready")
        v_saved, logits_saved = sem("v_saved"), sem("logits_saved")
        parts_out = [sem(f"parts_out{s}") for s in range(2)]
        route = sem("route")
        counted = sem("counted")
        gate_exp = sem("gate_exp")
        placed = sem("placed")
        scattered = sem("scattered")
        stacks_in = [sem(f"stacks_in{s}") for s in range(2)]
        residual_in = sem("residual_in")
        kf_ps, kf_ready = sem("kf_ps"), sem("kf_ready")
        qf_ps, qf_ready = sem("qf_ps"), sem("qf_ready")
        kv_ps, kv_ready = sem("kv_ps"), sem("kv_ready")
        v_spread = sem("v_spread")
        kvT_ps, kv_split = sem("kvT_ps"), sem("kv_split")
        o_ps, o_saved, attn_ready = sem("o_ps"), sem("o_saved"), sem("attn_ready")
        inv_ready = sem("inv_ready")
        wo_ps, r_ready = sem("wo_ps"), sem("r_ready")
        slot_in = [sem(f"slot_in{u}") for u in range(RING)]
        xsT_ps, xs_hi, xs_lo = sem("xsT_ps"), sem("xs_hi"), sem("xs_lo")
        gate_saved = sem("gate_saved")
        hid_ps, hid_ready = sem("hid_ps"), sem("hid_ready")
        hidT_ps, hidT_ready = sem("hidT_ps"), sem("hidT_ready")
        y_ps, y_ready, id_ready = sem("y_ps"), sem("y_ready"), sem("id_ready")
        y_out = [sem(f"y_out{u}") for u in range(RING)]
        y_back = [sem(f"y_back{n}") for n in range(SUMS)]
        summed = sem("summed")
        out_done = sem("out_done")

        x_b = x.rearrange("b (p k) d -> b p (k d)", k=K)
        out_b = out.rearrange("b (p k) d -> b p (k d)", k=K)
        y_b = expert_y.rearrange("(b p k) d -> b p (k d)", p=P, k=K)

        def strided(ap, dims):
            return bass.AP(ap.tensor, ap.offset, [list(ap.ap[0])] + [list(d) for d in dims])

        def due(eng, s, n):
            if not isinstance(n, int) or n > 0:
                eng.wait_ge(s, n)

        block = ctx.enter_context(nc.Block())

        @block.sync
        def _(sp):
            def load_x(c, s):
                sp.dma_start(x_ring[s].rearrange("p (b n) -> p b n", b=CHUNK),
                             x_b[bass.ds(CHUNK * c, CHUNK)].rearrange("b p n -> p b n")).then_inc(x_loaded[s], 16)

            load_x(0, 0)
            sp.wait_ge(zeroed, 1)
            for part in (0, 64, 96):
                for at, n, src in ((0, D, bv), (D, E, br), (VW, D, bo)):
                    sp.dma_start(bias_f[part:part + 1, at:at + n], src.rearrange("(a n) -> a n", a=1)) \
                        .then_inc(bias_in, 16)
            for dst, src in ((wq_sb[:, :], Wq), (wk_sb[:, :], Wk), (wvr_sb[:, 0:D], Wv), (wvr_sb[:, D:VW], wr),
                             (bq_col[:, :], bq.rearrange("(p a) -> p a", a=1)),
                             (bk_col[:, :], bk.rearrange("(p a) -> p a", a=1)), (wo_sb[:, :], Wo)):
                sp.dma_start(dst, src).then_inc(wts_in, 16)
            load_x(1, 1)
            sp.wait_ge(zeroed, 2)
            rw_h = rw.rearrange("(g h) d f -> h d g f", h=GH)
            for t in range(4):
                for hh in range(GH):
                    r0 = t * GD + hh * DK
                    sp.dma_start(rw_f[r0:r0 + DK, :, hh * F:(hh + 1) * F], rw_h[hh]).then_inc(rw_in, 16)
            sp.wait_ge(zeroed, 3)
            sp.dma_start(sorted_x.rearrange("(j p) w -> p j w", p=P),
                         strided(ones_f[:, :], [(0, SLOT_TILES), (1, XW)])).then_inc(filled, 16)

            def save_rows(c, s, more):
                sp.wait_ge(xn_ready, c + 1)
                sp.dma_start(rows_all[:, bass.ds(CHUNK * K * c, CHUNK * K), 0:D],
                             xn_ring[s].rearrange("p (t d) -> p t d", d=D)).then_inc(rows_saved[s], 16)
                if more:
                    load_x(c + 2, s)

            def save_parts(c, s):
                sp.wait_ge(lo_ready, 2 * c + 2)
                for n, dram in ((0, q_parts), (1, k_parts)):
                    for h in range(2):
                        sp.dma_start(dram[bass.ds(CHUNK * c, CHUNK), h].rearrange("b p n -> p b n"),
                                     qk_part[n][h][s].bitcast(F32).rearrange("p (b n) -> p b n", b=CHUNK)).then_inc(parts_out[s], 16)

            save_rows(0, 0, True)
            with sp.Fori(0, CHUNKS // 2 - 2) as i:
                for s in range(2):
                    save_rows(2 * i + s + 1, 1 - s, True)
                    save_parts(2 * i + s, s)
            save_rows(CHUNKS - 3, 1, True)
            save_parts(CHUNKS - 4, 0)
            save_rows(CHUNKS - 2, 0, False)
            save_parts(CHUNKS - 3, 1)
            save_rows(CHUNKS - 1, 1, False)
            save_parts(CHUNKS - 2, 0)
            save_parts(CHUNKS - 1, 1)
            for s in range(2):
                sp.wait_ge(parts_out[s], 64 * (CHUNKS // 2))
            sp.wait_ge(v_saved, NBATCH)

            def load_stacks(b, s):
                for t in range(4):
                    for stack, dram in ((q_stack, q_parts), (k_stack, k_parts)):
                        sp.dma_start(stack[s][t * GD:(t + 1) * GD, :, :].bitcast(F32),
                                     dram[b, t // 2].rearrange("(g p) n -> p g n", g=G)).then_inc(stacks_in[s], 16)

            for s in range(2):
                load_stacks(s, s)
            sp.dma_start(r_all[:, :, :], x_b.rearrange("b p n -> p b n")).then_inc(residual_in, 16)
            with sp.Fori(0, NBATCH // 2 - 1) as i:
                for s in range(2):
                    sp.wait_ge(qf_ps, 4 * i + 2 * s + 2)
                    load_stacks(2 * i + s + 2, s)

            sp.wait_ge(scattered, 16 * TILES)

            def load_slot(j, u):
                sp.dma_start(slot_rows[u][:, :], sorted_x[bass.ds(j * P, P), :]).then_inc(slot_in[u], 16)

            for u in range(RING):
                load_slot(u, u)
            with sp.Fori(0, SLOT_TILES // RING - 1) as i:
                for u in range(RING):
                    sp.wait_ge(xsT_ps, RING * i + u + 1)
                    sp.wait_ge(gate_saved, RING * i + u + 1)
                    load_slot(RING * i + u + RING, u)

            for u in range(RING):
                sp.wait_ge(y_out[u], 16 * (SLOT_TILES // RING))
            BS = NBATCH // SUMS
            for n in range(SUMS):
                sp.dma_start(y_all[:, BS * n:BS * (n + 1), :], y_b[BS * n:BS * (n + 1)].rearrange("b p n -> p b n")) \
                    .then_inc(y_back[n], 16)
            for n in range(SUMS):
                sp.wait_ge(summed, n + 1)
                sp.dma_start(out_b[BS * n:BS * (n + 1)].rearrange("b p n -> p b n"), r_all[:, BS * n:BS * (n + 1), :]) \
                    .then_inc(out_done, 16)
            sp.wait_ge(out_done, 16 * SUMS)

        @block.gpsimd
        def _(pool):
            steps = [0]

            def then(ins):
                steps[0] += 1
                ins.then_inc(pool_step, 1)
                pool.wait_ge(pool_step, steps[0])

            pool.memset(ln_eps[:, :], LN_EPS).then_inc(eps_ready, 1)
            pool.memset(bias_f[:, :], 0.0).then_inc(zeroed, 1)
            then(pool.memset(ident[:, :], 0.0))
            pool.memset(ones_b[:, :], 1.0).then_inc(consts_ready, 1)
            pool.affine_select(out=ident[:, :], in_=ident[:, :], compare_op=ALU.not_equal, fill=1.0, base=0,
                               pattern=[[-1, P]], channel_multiplier=1).then_inc(consts_ready, 1)
            pool.memset(rw_f, 0.0).then_inc(zeroed, 1)
            pool.memset(ones_f[:, :], 1.0).then_inc(zeroed, 1)

            def normalise(c, s):
                pool.wait_ge(rstd_ready, c + 1)
                due(pool, xnT_ps, c - 1)
                due(pool, rows_saved[s], 16 * (c // 2))
                for t in range(CHUNK * K):
                    ins = pool.tensor_scalar(xn_ring[s][:, t * D:(t + 1) * D], x_ring[s][:, t * D:(t + 1) * D],
                                             meanvar[s][:, t, 0:1], rstd[s][:, t:t + 1], ALU.subtract, ALU.mult)
                ins.then_inc(xn_ready, 1)

            for c in range(CHUNKS):
                normalise(c, c % 2)

            then(pool.memset(before[:, :], 1.0))
            pool.affine_select(out=before[:, :], in_=before[:, :], compare_op=ALU.is_gt, fill=0.0, base=0,
                               pattern=[[1, P]], channel_multiplier=-1).then_inc(mask_ready, 1)
            then(pool.memset(keep[:, :, :], 1.0))
            pool.memset(keep[:, :, 0:1], 0.0).then_inc(mask_ready, 1)
            then(pool.iota(rank_i[:, :, :], [[0, TILES], [-1, E]], base=E, channel_multiplier=0))
            pool.tensor_copy(rank_w[:, :, :], rank_i[:, :, :]).then_inc(mask_ready, 1)
            then(pool.iota(slot_no_i[:, :], [[1, SLOT_TILES]], base=0, channel_multiplier=0))
            pool.tensor_copy(slot_no[:, :], slot_no_i[:, :]).then_inc(mask_ready, 1)
            pool.iota(head_bit_i[:, :], [[0, 1]], base=0, channel_multiplier=1).then_inc(mask_ready, 1)
            pool.iota(rows_all[:, :, D + 1:XW].bitcast(I32), [[K * P, NBATCH], [1, K]], base=0, channel_multiplier=K) \
                .then_inc(mask_ready, 1)
            for s in range(2):
                pool.memset(k_feat[s][:, :, :, P:P + 1], EPS).then_inc(mask_ready, 1)
                pool.memset(v_ones[s][:, :, :, HD:], 1.0).then_inc(mask_ready, 1)
                pool.memset(kv_num[s][:, :, :], 0.0).then_inc(mask_ready, 1)
                pool.memset(kv_den[s][:, :, :], 0.0).then_inc(mask_ready, 1)

            pool.wait_ge(placed, 2)
            for s in range(2):
                pool.wait_ge(rows_saved[s], 16 * (CHUNKS // 2))
            pool.wait_ge(filled, 16)
            pool.wait_ge(mask_ready, 14)
            for t in range(TILES):
                pool.indirect_dma_start(sorted_x, bass.IndirectOffsetOnAxis(ap=place_i[:, t:t + 1], axis=0),
                                        rows_all[:, t, :], None).then_inc(scattered, 16)

            pool.wait_ge(scattered, 16 * TILES)
            pool.dma_start(w2_sb.rearrange("p (e a d) -> p e a d", e=E, a=IB),
                           w2.rearrange("e (a p) d -> p e a d", p=P)).then_inc(w2_in, 16)
            ES = STAGE // I
            loads = [0]

            def staged(*pairs):
                for dst, src in pairs:
                    pool.dma_start(dst, src).then_inc(stage_in, 16)
                    loads[0] += 16
                pool.wait_ge(stage_in, loads[0])

            for n in range(E // ES):
                c = slice(n * STAGE, (n + 1) * STAGE)
                staged((stage[0].rearrange("p (e n) -> p e n", e=ES),
                        w1[n * ES:(n + 1) * ES].rearrange("e p n -> p e n")))
                then(pool.tensor_copy(w1_hi[:, c], stage[0]))
                then(pool.tensor_tensor(w1_lo[:, c], stage[0], w1_hi[:, c], ALU.subtract))
            then(pool.memset(stage[0], 0.0))
            for n in range(E // ES):
                c = slice(n * STAGE, (n + 1) * STAGE)
                src = b1[n * ES:(n + 1) * ES].rearrange("(a e) n -> a (e n)", a=1)
                staged((stage[0][0:1, :], src), (stage[0][64:65, :], src))
                then(pool.tensor_copy(b1_rows[:, c], stage[0]))
                then(pool.tensor_tensor(b1_rows[64:P, c], stage[0][64:P, :], b1_rows[64:P, c], ALU.subtract))
            src = b2.rearrange("(a e) n -> a (e n)", a=1)
            staged(*((stage[0][r:r + 1, :], src) for r in (0, 64, 96)))
            then(pool.tensor_copy(b2_rows[:, :], stage[0]))
            then(pool.tensor_tensor(stage[1][64:P, :], stage[0][64:P, :], b2_rows[64:P, :], ALU.subtract))
            then(pool.tensor_copy(b2_rows[64:P, :], stage[1][64:P, :]))
            then(pool.tensor_tensor(stage[1][96:P, :], stage[1][96:P, :], b2_rows[96:P, :], ALU.subtract))
            pool.tensor_copy(b2_rows[96:P, :], stage[1][96:P, :]).then_inc(experts_ready, 1)

            def put(j, u):
                pool.wait_ge(y_ready, j + 1)
                pool.wait_ge(id_ready, j + 1)
                pool.indirect_dma_start(expert_y, bass.IndirectOffsetOnAxis(ap=row_id[u][:, :].bitcast(I32), axis=0),
                                        y_gated[u][:, :], None, bounds_check=ROWS - 1, oob_is_err=False) \
                    .then_inc(y_out[u], 16)

            for j in range(SLOT_TILES):
                put(j, j % RING)

        @block.tensor
        def _(pe):
            def turn(c, s):
                pe.wait_ge(xn_ready, c + 1)
                due(pe, xnT_ready, c)
                for t in range(CHUNK * K):
                    ins = pe.transpose(xnT_bank[:, t * P:(t + 1) * P], xn_ring[s][:, t * D:(t + 1) * D], ident[:, :])
                ins.then_inc(xnT_ps, 1)

            def project(c, s, more):
                pe.wait_ge(xnT_ready, c + 1)
                due(pe, lo_ready, 2 * c - 1)
                pe.matmul(q_bank, wq_sb[:, :], xnT[s], start=True, stop=True).then_inc(qk_ps, 1)
                if more:
                    turn(c + 1, 1 - s)
                due(pe, lo_ready, 2 * c)
                pe.matmul(k_bank, wk_sb[:, :], xnT[s], start=True, stop=True).then_inc(qk_ps, 1)
                for h in range(CHUNK):
                    due(pe, logits_saved, 2 * c - 1 + h)
                    for k in range(K):
                        t = K * h + k
                        pe.matmul(v_bank[h][:, k, :], ones_b[:, :], bias_vr, start=True, stop=False)
                        ins = pe.matmul(v_bank[h][:, k, :], xnT[s][:, t * P:(t + 1) * P], wvr_sb[:, :],
                                        start=False, stop=True)
                    ins.then_inc(v_ps, 1)

            pe.wait_ge(consts_ready, 2)
            turn(0, 0)
            pe.wait_ge(wts_in, 16 * 7)
            pe.wait_ge(bias_ready, 1)
            project(0, 0, True)
            project(1, 1, True)
            with pe.Fori(1, CHUNKS // 2 - 1) as i:
                for s in range(2):
                    project(2 * i + s, s, True)
            project(CHUNKS - 2, 0, True)
            project(CHUNKS - 1, 1, False)

            pe.wait_ge(mask_ready, 6)
            pe.wait_ge(route, R_EARLIER)
            pe.matmul(rank_bank, before[:, :], onehot[:, :, :], start=True, stop=False)
            pe.matmul(rank_bank, ones_b[:, :], earlier[:, :, :], start=False, stop=True).then_inc(counted, 1)
            pe.matmul(count_bank, ones_b[:, :], strided(upto[:, 0, TILES - 1:TILES], [(TILES, E)]),
                      start=True, stop=True).then_inc(counted, 1)

            def k_features(b, s, k):
                due(pe, qf_ready, 2 * b - 1 + k)
                for g in range(G):
                    ins = pe.matmul(pair[k][:, g * GH * F:(g + 1) * GH * F], k_stack[s][:, g, k * P:(k + 1) * P],
                                    rw_stack[:, g, :], start=True, stop=True)
                ins.then_inc(kf_ps, 1)

            def q_features(b, s, h):
                pe.wait_ge(kf_ready, 2 * b + 1 + h)
                for c in range(h * NC // 2, (h + 1) * NC // 2):
                    g, half = c // 2, c % 2
                    m = c % (NC // 2)
                    ins = pe.matmul(pair[h][:, m * S:(m + 1) * S], rw_stack[:, g, half * P:(half + 1) * P],
                                    q_stack[s][:, g, :], start=True, stop=True)
                ins.then_inc(qf_ps, 1)

            def key_values(b, s):
                pe.wait_ge(kf_ready, 2 * b + 2)
                pe.wait_ge(v_spread, b + 1)
                due(pe, kv_ready, 2 * b)
                for par in range(2):
                    for k in range(K):
                        for j in range(NC // 2):
                            c = 2 * j + par
                            ins = pe.matmul(kv_bank[GD * j:GD * (j + 1), par, :], v_ones[s][:, k, c, :],
                                            k_feat[s][:, k, c, :], start=(k == 0), stop=(k == K - 1))
                ins.then_inc(kv_ps, 1)

            def turn_kv(b):
                pe.wait_ge(kv_ready, 2 * b + 2)
                due(pe, kv_split, 2 * b)
                for par in range(2):
                    ins = pe.transpose(kvT_bank[:, par, :], kv_T[:, par, :], ident[:, :])
                ins.then_inc(kvT_ps, 1)

            def outputs(b, s):
                pe.wait_ge(kv_split, 2 * b + 2)
                pe.wait_ge(qf_ready, 2 * b + 2)
                due(pe, o_saved, 2 * b)
                for n, kv in ((0, kv_num), (1, kv_den)):
                    for par in range(2):
                        for j in range(NC // 2):
                            c = 2 * j + par
                            ins = pe.matmul(o_bank[GD * j:GD * (j + 1), n * S:(n + 1) * S], kv[s][:, c, :],
                                            q_feat[s][:, c, :], start=(par == 0), stop=(par == 1))
                ins.then_inc(o_ps, 1)

            def out_project(b, s):
                pe.wait_ge(attn_ready, b + 1)
                due(pe, r_ready, b)
                for k in range(K):
                    pe.matmul(wo_bank[:, k * D:(k + 1) * D], ones_b[:, :], bias_o, start=True, stop=False)
                    ins = pe.matmul(wo_bank[:, k * D:(k + 1) * D], attn_T[s][:, k * P:(k + 1) * P], wo_sb[:, :],
                                    start=False, stop=True)
                ins.then_inc(wo_ps, 1)

            def batch(b, s, i, before_it=2):
                pe.wait_ge(stacks_in[s], STACK_LOADS * (i + 1))
                k_features(b, s, 0)
                if before_it >= 1:
                    turn_kv(b - 1)
                k_features(b, s, 1)
                if before_it >= 1:
                    outputs(b - 1, 1 - s)
                for h in range(2):
                    q_features(b, s, h)
                key_values(b, s)
                if before_it >= 2:
                    out_project(b - 2, s)

            pe.wait_ge(rw_ready, 2)
            pe.wait_ge(mask_ready, 14)
            pe.wait_ge(placed, 1)
            for b in range(4):
                batch(b, b % 2, b // 2, before_it=b)
            with pe.Fori(2, NBATCH // 2) as i:
                for s in range(2):
                    batch(2 * i + s, s, i)
            turn_kv(NBATCH - 1)
            out_project(NBATCH - 2, 0)
            outputs(NBATCH - 1, 1)
            out_project(NBATCH - 1, 1)

            def turn_slot(j, u, n):
                pe.wait_ge(slot_in[u], 16 * (n + 1))
                due(pe, xs_hi, j)
                due(pe, xs_lo, j)
                pe.transpose(xsT_bank, slot_rows[u][:, 0:D], ident[:, :]).then_inc(xsT_ps, 1)

            up_reg, down_reg = pe.alloc_register("up_expert"), pe.alloc_register("down_expert")

            def read_expert(reg, j):
                pe.reg_load(reg, expert_no[0:1, bass.ds(j, 1)])

            def expert_in(reg):
                return pe.snap(reg, min_val=0, max_val=E - 1)

            def up(j, u):
                e = expert_in(up_reg)
                pe.wait_ge(xs_hi, j + 1)
                pe.wait_ge(xs_lo, j + 1)
                due(pe, hid_ready, j - 2)
                w = bass.ds(e * I, I)
                pe.matmul(hid_bank[u], ones_r[:, :], b1_rows[:, w], start=True, stop=False)
                pe.matmul(hid_bank[u], xsT_hi[u][:, :], w1_hi[:, w], start=False, stop=False)
                pe.matmul(hid_bank[u], xsT_hi[u][:, :], w1_lo[:, w], start=False, stop=False)
                pe.matmul(hid_bank[u], xsT_lo[u][:, :], w1_hi[:, w], start=False, stop=True).then_inc(hid_ps, 1)

            def turn_hidden(j, u):
                pe.wait_ge(hid_ready, j + 1)
                due(pe, hidT_ready, j - 2)
                for a in range(IB):
                    ins = pe.transpose(hidT_bank[u][:, a * P:(a + 1) * P], hidden[u][:, a * P:(a + 1) * P], ident[:, :])
                ins.then_inc(hidT_ps, 1)

            def down(j, u):
                e = expert_in(down_reg)
                pe.wait_ge(hidT_ready, j + 1)
                due(pe, y_ready, j)
                pe.matmul(y_bank, ones_b[:, :], b2_rows[:, bass.ds(e * D, D)], start=True, stop=False)
                for a in range(IB):
                    ins = pe.matmul(y_bank, hidden_T[u][:, a * P:(a + 1) * P], w2_sb[:, bass.ds(e * IB * D + a * D, D)],
                                    start=False, stop=(a == IB - 1))
                ins.then_inc(y_ps, 1)

            def slot_tile(j, u, n, first=False, last=False):
                up(j, u)
                if not last:
                    read_expert(up_reg, j + 1)
                if not first or u >= 2:
                    read_expert(down_reg, j - 2)
                if not last:
                    turn_slot(j + 1, (u + 1) % RING, n + (u + 1) // RING)
                if not first or u >= 1:
                    turn_hidden(j - 1, (u - 1) % RING)
                if not first or u >= 2:
                    down(j - 2, (u - 2) % RING)

            pe.wait_ge(ones_ready, 1)
            pe.wait_ge(experts_ready, 1)
            pe.wait_ge(w2_in, 16)
            pe.wait_ge(placed, 3)
            pe.wait_ge(r_ready, NBATCH)
            read_expert(up_reg, 0)
            turn_slot(0, 0, 0)
            for u in range(RING):
                slot_tile(u, u, 0, first=True)
            for u in range(RING):
                slot_tile(RING + u, u, 1)
            with pe.Fori(2, SLOT_TILES // RING - 1) as i:
                for u in range(RING):
                    slot_tile(RING * i + u, u, i)
            n = SLOT_TILES // RING - 1
            for u in range(RING):
                slot_tile(RING * n + u, u, n, last=(u == RING - 1))
            turn_hidden(SLOT_TILES - 1, RING - 1)
            read_expert(down_reg, SLOT_TILES - 2)
            down(SLOT_TILES - 2, RING - 2)
            read_expert(down_reg, SLOT_TILES - 1)
            down(SLOT_TILES - 1, RING - 1)

        @block.scalar
        def _(act):
            def save_xnT(c, s):
                act.wait_ge(xnT_ps, c + 1)
                due(act, v_ps, 2 * c - 2)
                act.activation(xnT[s], xnT_bank, ACT.Copy).then_inc(xnT_ready, 1)

            def split_hi(c, s, n):
                bank, bias = ((q_bank, bq_col), (k_bank, bk_col))[n]
                act.wait_ge(qk_ps, 2 * c + n + 1)
                act.activation(qk_part[n][0][s], bank, ACT.Identity,
                               bias=bias[:, 0:1]).then_inc(hi_ready, 1)

            def deviation(c, s):
                act.wait_ge(mv_ready, c + 1)
                due(act, rstd_ready, c - 1)
                act.activation(std[s][:, :], meanvar[s][:, :, 1], ACT.Sqrt, bias=ln_eps[:, 0:1]).then_inc(std_ready, 1)

            def chunk(c, s, i, more=True, ahead=True):
                if not isinstance(c, int) or c >= 2:
                    act.wait_ge(parts_out[s], 64 * i)
                split_hi(c, s, 0)
                if ahead:
                    deviation(c + 2, s)
                if more:
                    save_xnT(c + 1, 1 - s)
                split_hi(c, s, 1)
                for h in range(CHUNK):
                    act.wait_ge(v_ps, 2 * c + h + 1)
                    act.activation(v_all[:, CHUNK * c + h, :].rearrange("p (k d) -> p k d", k=K),
                                   v_bank[h][:, :, 0:D], ACT.Copy).then_inc(v_saved, 1)

            act.wait_ge(eps_ready, 1)
            deviation(0, 0)
            deviation(1, 1)
            act.wait_ge(wts_in, 16 * 7)
            save_xnT(0, 0)
            chunk(0, 0, 0, True)
            chunk(1, 1, 0, True)
            with act.Fori(1, CHUNKS // 2 - 1) as i:
                for s in range(2):
                    chunk(2 * i + s, s, i, True)
            chunk(CHUNKS - 2, 0, CHUNKS // 2 - 1, ahead=False)
            chunk(CHUNKS - 1, 1, CHUNKS // 2 - 1, more=False, ahead=False)

            act.wait_ge(route, R_GATE)
            act.activation(gate_e[:, :], gate_d[:, :], ACT.Exp).then_inc(gate_exp, 1)

            def k_relu(b, s, k):
                act.wait_ge(kf_ps, 2 * b + 1 + k)
                due(act, kv_ps, b - 1)
                act.activation(k_feat[s][:, k, :, 0:P], pair[k][:, :].rearrange("p (c n) -> p c n", c=NC), ACT.Relu) \
                    .then_inc(kf_ready, 1)

            def save_outputs(b, s):
                act.wait_ge(o_ps, b + 1)
                due(act, attn_ready, b - 1)
                act.activation(den[s][:, :], o_bank[:, S:2 * S], ACT.Copy, bias=EPS).then_inc(o_saved, 1)
                act.activation(num[s][:, :], o_bank[:, 0:S], ACT.Copy).then_inc(o_saved, 1)

            def split_kv(b, s):
                act.wait_ge(kvT_ps, b + 1)
                due(act, o_ps, b - 1)
                for n, kv in ((0, kv_num), (1, kv_den)):
                    act.activation(strided(kv[s][:, 0, 0:1], [(GD + 16, 2), (2 * GD, NC // 2), (1, 16)]),
                                   strided(kvT_bank[:, 0, 16 * n:16 * n + 1], [(P, 2), (GD, NC // 2), (1, 16)]),
                                   ACT.Copy).then_inc(kv_split, 1)

            def spread_v(b, s):
                due(act, kv_ps, b - 1)
                act.activation(v_ones[s][:, :, :, 0:HD].rearrange("p k c d -> p (k c) d"),
                               v_all[:, b, :].rearrange("p (m d) -> p m d", d=HD), ACT.Copy).then_inc(v_spread, 1)

            def batch(b, s, first=False, last=False):
                k_relu(b, s, 0)
                if not first:
                    split_kv(b - 1, 1 - s)
                k_relu(b, s, 1)
                if not first:
                    save_outputs(b - 1, 1 - s)
                if not last:
                    spread_v(b + 1, 1 - s)

            act.wait_ge(mask_ready, 14)
            act.wait_ge(v_saved, NBATCH)
            spread_v(0, 0)
            batch(0, 0, first=True)
            for b in range(1, 4):
                batch(b, b % 2)
            with act.Fori(2, NBATCH // 2 - 1) as i:
                for s in range(2):
                    batch(2 * i + s, s)
            batch(NBATCH - 2, 0)
            batch(NBATCH - 1, 1, last=True)
            split_kv(NBATCH - 1, 1)
            save_outputs(NBATCH - 1, 1)

            def gelu(j, u):
                act.wait_ge(hid_ps, j + 1)
                due(act, hidT_ps, j - 2)
                act.activation(hidden[u][:, :], hid_bank[u], ACT.Gelu).then_inc(hid_ready, 1)

            def slot_hi(j, u):
                act.wait_ge(xsT_ps, j + 1)
                due(act, hid_ps, j - 2)
                act.activation(xsT_hi[u][:, :], xsT_bank, ACT.Copy).then_inc(xs_hi, 1)

            slot_hi(0, 0)
            for u in range(RING):
                gelu(u, u)
                slot_hi(u + 1, (u + 1) % RING)
            with act.Fori(1, SLOT_TILES // RING - 1) as i:
                for u in range(RING):
                    gelu(RING * i + u, u)
                    slot_hi(RING * i + u + 1, (u + 1) % RING)
            for u in range(RING):
                j = SLOT_TILES - RING + u
                gelu(j, u)
                if u < RING - 1:
                    slot_hi(j + 1, u + 1)

        @block.vector
        def _(dve):
            BV = slice(64, P)
            dve.wait_ge(bias_in, 16 * 9)
            dve.tensor_copy(bias_vro[:, :], bias_f[:, :]).then_inc(bias_split, 1)
            dve.wait_ge(bias_split, 1)
            dve.tensor_tensor(bias_f[BV, :], bias_f[BV, :], bias_vro[BV, :], ALU.subtract).then_inc(bias_split, 1)
            dve.wait_ge(bias_split, 2)
            dve.tensor_copy(bias_vro[BV, :], bias_f[BV, :]).then_inc(bias_split, 1)
            dve.wait_ge(bias_split, 3)
            dve.tensor_tensor(bias_f[96:P, :], bias_f[96:P, :], bias_vro[96:P, :], ALU.subtract).then_inc(bias_split, 1)
            dve.wait_ge(bias_split, 4)
            dve.tensor_copy(bias_vro[96:P, :], bias_f[96:P, :]).then_inc(bias_ready, 1)

            def row_stats(c, s, i):
                dve.wait_ge(x_loaded[s], 16 * (i + 1))
                due(dve, mv_ready, c)
                for t in range(CHUNK * K):
                    ins = dve.bn_stats(stats[:, t, :], x_ring[s][:, t * D:(t + 1) * D])
                ins.then_inc(stats_ready, 1)
                dve.wait_ge(stats_ready, c + 1)
                due(dve, xn_ready, c - 1)

            def row_moments(c, s):
                for t in range(CHUNK * K):
                    ins = dve.bn_aggr(meanvar[s][:, t, :], stats[:, t, :])
                ins.then_inc(mv_ready, 1)

            def row_scale(c, s):
                dve.wait_ge(std_ready, c + 1)
                due(dve, xn_ready, c - 1)
                dve.reciprocal(rstd[s][:, :], std[s][:, :]).then_inc(rstd_ready, 1)

            def split_lo(c, s, n):
                bank, bias = ((q_bank, bq_col), (k_bank, bk_col))[n]
                dve.wait_ge(hi_ready, 2 * c + n + 1)
                hi, lo = qk_part[n][0][s], qk_part[n][1][s]
                dve.scalar_tensor_tensor(out=lo, in0=bank, scalar=bias[:, 0:1], in1=hi.bitcast(F32), op0=ALU.add,
                                         op1=ALU.subtract).then_inc(lo_ready, 1)

            def save_logits(c, h):
                dve.wait_ge(v_saved, 2 * c + h + 1)
                dve.tensor_copy(logits[:, bass.ds(K * (CHUNK * c + h), K), :], v_bank[h][:, :, D:VW]) \
                    .then_inc(logits_saved, 1)

            def chunk(c, s, i, ahead=True):
                if ahead:
                    row_stats(c + 2, s, i + 1)
                if not isinstance(c, int) or c >= 2:
                    dve.wait_ge(parts_out[s], 64 * i)
                split_lo(c, s, 0)
                if ahead:
                    row_moments(c + 2, s)
                    row_scale(c + 2, s)
                split_lo(c, s, 1)
                for h in range(CHUNK):
                    save_logits(c, h)

            row_stats(0, 0, 0)
            row_moments(0, 0)
            row_scale(0, 0)
            row_stats(1, 1, 0)
            row_moments(1, 1)
            row_scale(1, 1)
            dve.wait_ge(wts_in, 16 * 7)
            chunk(0, 0, 0, True)
            chunk(1, 1, 0, True)
            with dve.Fori(1, CHUNKS // 2 - 1) as i:
                for s in range(2):
                    chunk(2 * i + s, s, i, True)
            chunk(CHUNKS - 2, 0, CHUNKS // 2 - 1, ahead=False)
            chunk(CHUNKS - 1, 1, CHUNKS // 2 - 1, ahead=False)

            dve.wait_ge(rw_in, 16 * 16)
            dve.tensor_copy(rw_stack[:, :, :], rw_f).then_inc(rw_split, 1)
            dve.wait_ge(rw_split, 1)
            for r in (slice(GD, 2 * GD), slice(3 * GD, 4 * GD)):
                dve.tensor_tensor(rw_stack[r, :, :], rw_f[r, :, :], rw_stack[r, :, :].bitcast(F32), ALU.subtract) \
                    .then_inc(rw_ready, 1)

            steps = [0]

            def then(ins):
                steps[0] += 1
                ins.then_inc(route, 1)
                dve.wait_ge(route, steps[0])

            dve.wait_ge(logits_saved, NBATCH)
            dve.wait_ge(mask_ready, 6)
            for t in range(TILES):
                ins = dve.max(top8[:, t, :], logits[:, t, :])
            then(ins)
            dve.tensor_tensor(gate_d[:, :], top8[:, :, 1], top8[:, :, 0], ALU.subtract).then_inc(route, 1)
            steps[0] += 1
            assert steps[0] == R_GATE
            then(dve.tensor_tensor(is_top[:, :, :], logits[:, :, :], strided(top8[:, 0, 0:1], [(E, TILES), (0, E)]),
                                   ALU.is_equal))
            then(dve.tensor_tensor(is_top[:, :, :], is_top[:, :, :], rank_w[:, :, :], ALU.mult))
            then(dve.tensor_reduce(top_w[:, :], is_top[:, :, :], AX.X, ALU.max))
            then(dve.tensor_tensor(onehot[:, :, :].rearrange("p e t -> p t e"), is_top[:, :, :],
                                   strided(top_w[:, 0:1], [(1, TILES), (0, E)]), ALU.is_equal))
            flat = lambda m: m[:, :, :].rearrange("p e t -> p (e t)")
            then(dve.tensor_tensor_scan(flat(upto), flat(keep), flat(onehot), 0.0, ALU.mult, ALU.add))
            then(dve.tensor_tensor(earlier[:, :, :], upto[:, :, :], onehot[:, :, :], ALU.subtract))
            assert steps[0] == R_EARLIER
            dve.wait_ge(counted, 2)
            then(dve.tensor_scalar(cnt_i[:, :], count_bank, float(P - 1), None, ALU.add))
            then(dve.tensor_scalar(tiles_i[:, :], cnt_i[:, :], 7, None, ALU.arith_shift_right))
            then(dve.tensor_copy(tiles_f[:, :], tiles_i[:, :]))
            then(dve.tensor_tensor_scan(tiles_upto[:, :], ones_f[:, 0:E], tiles_f[:, :], 0.0, ALU.mult, ALU.add))
            then(dve.tensor_tensor(first_slot[:, :], tiles_upto[:, :], tiles_f[:, :], ALU.subtract))
            then(dve.tensor_scalar(first_slot[:, :], first_slot[:, :], float(P), None, ALU.mult))
            then(dve.tensor_tensor(place_a[:, :, :], rank_bank, strided(first_slot[:, 0:1], [(1, E), (0, TILES)]),
                                   ALU.add))
            then(dve.tensor_tensor(place_b[:, :, :], place_a[:, :, :], onehot[:, :, :], ALU.mult))
            then(dve.tensor_reduce(place_f[:, :], place_b[:, :, :].rearrange("p e t -> p t e"), AX.X, ALU.add))
            dve.tensor_copy(place_i[:, :], place_f[:, :]).then_inc(placed, 1)
            dve.wait_ge(gate_exp, 1)
            then(dve.tensor_scalar(gate_s[:, :], gate_e[:, :], 1.0, None, ALU.add))
            dve.reciprocal(rows_all[:, :, D], gate_s[:, :]).then_inc(placed, 1)
            then(dve.tensor_tensor(passed[:, :, :], strided(slot_no[:, 0:1], [(1, SLOT_TILES), (0, E)]),
                                   strided(tiles_upto[:, 0:1], [(0, SLOT_TILES), (1, E)]), ALU.is_ge))
            then(dve.tensor_reduce(expert_f[:, :], passed[:, :, :], AX.X, ALU.add))
            dve.tensor_scalar(expert_no[:, :], expert_f[:, :], float(E - 1), None, ALU.min).then_inc(placed, 1)
            then(dve.tensor_scalar(head_bit_i[:, :], head_bit_i[:, :], 3, 1, ALU.arith_shift_right, ALU.bitwise_and))
            then(dve.tensor_copy(head_bit[:, :], head_bit_i[:, :]))
            then(dve.tensor_copy(head_mask[:, F:P], strided(head_bit[:, 0:1], [(0, F)])))
            then(dve.tensor_scalar(head_mask[:, 0:F], head_mask[:, F:P], -1.0, 1.0, ALU.mult, ALU.add))
            dve.memset(ones_r[:, :].bitcast(F32), 1.0).then_inc(ones_ready, 1)

            def q_relu(b, s, h):
                dve.wait_ge(qf_ps, 2 * b + 1 + h)
                due(dve, o_ps, b - 1)
                dve.tensor_scalar(q_feat[s][:, h * NC // 2:(h + 1) * NC // 2, :].rearrange("p c n -> p (c n)"),
                                  pair[h][:, :], 0.0, EPS, ALU.max, ALU.add).then_inc(qf_ready, 1)

            def divide(b, s):
                dve.wait_ge(o_saved, 2 * b + 2)
                due(dve, wo_ps, b - 1)
                due(dve, attn_ready, b)
                dve.reciprocal(inv_den[:, :], den[s][:, :]).then_inc(inv_ready, 1)
                dve.wait_ge(inv_ready, b + 1)
                dve.tensor_tensor(attn_T[s][:, :], num[s][:, :], inv_den[:, :], ALU.mult).then_inc(attn_ready, 1)

            def mask_kv(b):
                dve.wait_ge(kv_ps, b + 1)
                due(dve, kvT_ps, b)
                for par in range(2):
                    dve.scalar_tensor_tensor(out=kv_T[:, par, :], in0=kv_bank[:, par, 0:P],
                                             scalar=kv_bank[:, par, P:P + 1], in1=head_mask[:, :],
                                             op0=ALU.add, op1=ALU.mult).then_inc(kv_ready, 1)

            def residual(b):
                dve.wait_ge(wo_ps, b + 1)
                dve.tensor_tensor(r_all[:, b, :], wo_bank[:, 0:K * D], r_all[:, b, :], ALU.add).then_inc(r_ready, 1)

            def batch(b, s, before_it=2):
                for h in range(2):
                    q_relu(b, s, h)
                mask_kv(b)
                if before_it >= 1:
                    divide(b - 1, 1 - s)
                if before_it >= 2:
                    residual(b - 2)

            dve.wait_ge(residual_in, 16)
            for b in range(4):
                batch(b, b % 2, before_it=b)
            with dve.Fori(2, NBATCH // 2) as i:
                for s in range(2):
                    batch(2 * i + s, s)
            divide(NBATCH - 1, 1)
            residual(NBATCH - 2)
            residual(NBATCH - 1)

            def slot_lo(j, u):
                dve.wait_ge(xs_hi, j + 1)
                due(dve, hid_ps, j - 2)
                dve.tensor_tensor(xsT_lo[u][:, :], xsT_bank, xsT_hi[u][:, :].bitcast(F32), ALU.subtract) \
                    .then_inc(xs_lo, 1)
                dve.tensor_copy(gate_id[:, j, :], slot_rows[u][:, D:XW]).then_inc(gate_saved, 1)

            def save_hidT(j, u):
                dve.wait_ge(hidT_ps, j + 1)
                due(dve, y_ps, j - 2)
                dve.tensor_copy(hidden_T[u][:, :], hidT_bank[u]).then_inc(hidT_ready, 1)

            def gate_y(j, u, n):
                dve.wait_ge(y_ps, j + 1)
                dve.wait_ge(gate_saved, j + 1)
                if not isinstance(n, int) or n >= 1:
                    dve.wait_ge(y_out[u], 16 * n)
                dve.tensor_copy(row_id[u][:, :], gate_id[:, j, 1:2]).then_inc(id_ready, 1)
                dve.tensor_scalar(y_gated[u][:, :], y_bank, gate_id[:, j, 0:1], None, ALU.mult).then_inc(y_ready, 1)

            def slot_tile(j, u, n, first=False, last=False):
                if not last:
                    slot_lo(j + 1, (u + 1) % RING)
                if not first or u >= 1:
                    save_hidT(j - 1, (u - 1) % RING)
                if not first or u >= 2:
                    gate_y(j - 2, (u - 2) % RING, n if u >= 2 else n - 1)

            slot_lo(0, 0)
            for u in range(RING):
                slot_tile(u, u, 0, first=True)
            for u in range(RING):
                slot_tile(RING + u, u, 1)
            with dve.Fori(2, SLOT_TILES // RING - 1) as i:
                for u in range(RING):
                    slot_tile(RING * i + u, u, i)
            n = SLOT_TILES // RING - 1
            for u in range(RING):
                slot_tile(RING * n + u, u, n, last=(u == RING - 1))
            save_hidT(SLOT_TILES - 1, RING - 1)
            gate_y(SLOT_TILES - 2, RING - 2, n)
            gate_y(SLOT_TILES - 1, RING - 1, n)

            BS = NBATCH // SUMS
            for n in range(SUMS):
                dve.wait_ge(y_back[n], 16)
                b = slice(BS * n, BS * (n + 1))
                dve.tensor_tensor(r_all[:, b, :], r_all[:, b, :], y_all[:, b, :], ALU.add).then_inc(summed, 1)


_NAMES = ["x", "Wq", "bq", "Wk", "bk", "Wv", "bv", "Wo", "bo", "rw", "w1", "b1", "w2", "b2", "wr", "br"]


def kernel(L0_attn_x, L0_attn_Wq, L0_attn_bq, L0_attn_Wk, L0_attn_bk, L0_attn_Wv, L0_attn_bv, L0_attn_Wo, L0_attn_bo,
           L0_attn_rw, L0_ffn_w1, L0_ffn_b1, L0_ffn_w2, L0_ffn_b2, L0_ffn_wr, L0_ffn_br):
    import numpy as np
    import concourse.bacc as bacc
    from concourse.bass_utils import run_bass_kernel_spmd

    given = [L0_attn_x, L0_attn_Wq, L0_attn_bq, L0_attn_Wk, L0_attn_bk, L0_attn_Wv, L0_attn_bv, L0_attn_Wo, L0_attn_bo,
             L0_attn_rw, L0_ffn_w1, L0_ffn_b1, L0_ffn_w2, L0_ffn_b2, L0_ffn_wr, L0_ffn_br]
    nc = bacc.Bacc("TRN2", target_bir_lowering=False, num_devices=1)
    arrays, args = {}, []
    for name, a in zip(_NAMES, given):
        a = np.ascontiguousarray(a)
        arrays[f"in_{name}"] = a
        args.append(nc.dram_tensor(f"in_{name}", a.shape, mybir.dt.from_np(a.dtype), kind="ExternalInput").ap())
    out = nc.dram_tensor("out", [NBATCH, S, D], F32, kind="ExternalOutput").ap()
    build(nc, *args, out)
    r = run_bass_kernel_spmd(nc, [arrays], core_ids=[0])
    return r.results[0]["out"]
```
